# Optimizing a Trainium2 kernel written in Bass

```python
import numpy as np
import jax
import jax.numpy as jnp

def _softmax(x, axis=-1):
    return jax.nn.softmax(x, axis=axis)

def _gelu(x):
    return jax.nn.gelu(x, approximate=True)

def _silu(x):
    return jax.nn.silu(x)

def _sigmoid(x):
    return jax.nn.sigmoid(x)

def _layernorm(x, axis=-1, eps=1e-05):
    m = jnp.mean(x, axis=axis, keepdims=True)
    v = jnp.var(x, axis=axis, keepdims=True)
    return (x - m) / jnp.sqrt(v + eps)

def _scatter_add(tgt, idx, src, axis=0):
    return tgt.at[idx].add(src)

def _segment_sum(src, seg, n):
    return jax.ops.segment_sum(src, seg, n)
kernel_name = 'mk_adj_resnorm_d1_adj_r2_40612c'

def setup_inputs(seed: int=0):
    np.random.seed(seed)
    _w = jnp.asarray

    def _rec_inputs():
        import jax
        import jax.numpy as jnp
        _gk = jax.random.key(seed)
        x = -0.0005207 + 1.001 * jax.random.normal(jax.random.fold_in(_gk, 1), (8192, 128), jnp.float32)
        _w = (1.0 + jnp.arange(8192, dtype=jnp.float32)) ** (-0.5)
        _w = _w / _w.mean()
        _pij = jnp.clip(0.00195312 * _w[:, None] * _w[None, :], 0.0, 1.0)
        _a = jax.random.uniform(jax.random.fold_in(_gk, 2), (8192, 8192)) < _pij
        _a = jnp.logical_or(_a, jnp.eye(8192, dtype=bool))
        _af = _a.astype(jnp.float32)
        _af = _af * jax.random.uniform(jax.random.fold_in(_gk, 3), (8192, 8192), jnp.float32, 0.05, 1)
        adj = _af
        return (x, adj)
    x, adj = _rec_inputs()

    def _L0_gnn_setup():
        import jax, jax.numpy as jnp
        import numpy as np
        N, IN_C, OUT_C = (4096, 128, 128)
        key = jax.random.key(seed)
        k1, k2, k3 = jax.random.split(key, 3)
        x = jax.random.normal(k1, (N, IN_C), dtype=jnp.float32)
        adj = jax.random.uniform(k2, (N, N), dtype=jnp.float32)
        w = jax.random.uniform(k3, (IN_C, OUT_C), dtype=jnp.float32)
        return {'x': x, 'adj': adj, 'w': w}
    _L0_gnn_all = _L0_gnn_setup()
    _L0_gnn_in = {k: v for k, v in _L0_gnn_all.items() if k in ('w',)}
    del _L0_gnn_all
    return {'x': x, 'adj': adj, 'L0_gnn_w': _L0_gnn_in['w']}

def reference(x, adj, L0_gnn_w):
    import jax
    import jax.numpy as jnp

    def _L0_gnn_ref(x, adj, w):
        import jax, jax.numpy as jnp
        import numpy as np
        N, IN_C, OUT_C = (4096, 128, 128)
        A = adj + jnp.eye(adj.shape[0], dtype=adj.dtype)
        deg = jnp.sum(A, axis=1)
        d_isqrt = jax.lax.rsqrt(deg)
        A_hat = A * d_isqrt[:, None] * d_isqrt[None, :]
        h = jnp.matmul(A_hat, x)
        return jax.nn.elu(jnp.matmul(h, w))
    x = _layernorm(x + _L0_gnn_ref(x, adj, L0_gnn_w), axis=-1)
    return x

_drawn_inputs = setup_inputs


def setup_inputs(seed=0):
    import zlib

    import numpy as np

    out = dict(_drawn_inputs(seed))
    spreads = {}
    factors = {}
    for name, (base, spread) in spreads.items():
        noise = np.random.default_rng([zlib.crc32(name.encode()), seed]).standard_normal(out[name].shape)
        drawn = base * np.exp(spread * noise) if base else spread * noise
        out[name] = jnp.asarray(drawn.astype(out[name].dtype))
    for name, factor in factors.items():
        out[name] = (out[name] * factor).astype(out[name].dtype)
    return out
```

```python
import concourse.bass as bass
from concourse import mybir
from contextlib import ExitStack

N = 8192
F = 128
NB = 16
B = N // NB
G = B // 32
Q = 4
CH = B // 128
SLOTS = 14
KEEP = 4
COLUMNS = [[n] for n in range(NB - 2)] + [[NB - 2, NB - 1]]
LEAD = 1
EPS = 1e-5


def plan():
    LOAD, PRODUCT, SUMS, TURN = 2.93, 3.42, 6.0, 2.2
    order, kept, read = [], set(), set()
    for cols in COLUMNS:
        for r in cols:
            inside = [t for t in cols if (r, t) not in read]
            later = [t for t in range(cols[-1] + 1, NB)]
            room = max(0, KEEP - sum(t > cols[-1] for _, t in kept))
            order += [("sum_only", r, t) for t in reversed(later[room:])]
            order += [("keep", r, t) for t in reversed(later[:room])] + [("keep", r, t) for t in inside]
            kept |= {(r, t) for t in inside + later[:room]}
            read |= {(r, t) for t in inside + later}
            order.append(("degree", r))
        rows = [s for s in range(NB) if all((s, t) in kept for t in cols)]
        rows += [s for s in range(cols[-1] + 1, NB)]
        rows += [s for s in range(NB) if s not in rows]
        for s in rows:
            for t in cols:
                if (s, t) not in kept:
                    order.append(("again" if (s, t) in read else "stream", s, t))
                    read.add((s, t))
            order.append(("product", s, cols))
        kept = {(s, t) for s, t in kept if t > cols[-1]}

    loads, at = [], {}
    pe_steps = []
    for o in order:
        if o[0] == "degree":
            back, here = 0, len(pe_steps)
            while here and back < LEAD and pe_steps[here - 1][0] != "degree":
                here -= 1
                back += 1
            while here and pe_steps[here - 1][0] == "degree" and back == 0:
                break
            pe_steps.insert(here if back else len(pe_steps), o)
        elif o[0] == "product":
            pe_steps.append(o)

    free = [(0.0, n) for n in range(SLOTS)]
    now, pe, last_first = 0.0, 0.0, {}
    ready, slot_of = {}, {}
    todo = list(pe_steps)
    vector, pool, products, done_at = [], [], [], {}

    def run_pe():
        nonlocal pe
        while todo:
            step = todo[0]
            if step[0] == "degree":
                if step[1] not in last_first:
                    return
                t0 = last_first[step[1]] + SUMS
                vector.append((t0, "row_sum", step[1]))
                pe = max(pe, t0 + 0.5) + 0.3
                vector.append((pe + 0.1, "degree", step[1]))
                pool.append((pe + 0.5, "power", step[1]))
                vector.append((pe + 1.0, "scale", step[1]))
                done_at[step[1]] = pe + 2.5
            else:
                _, s, cols = step
                if any((s, t) not in ready for t in cols) or any(t not in done_at for t in cols):
                    return
                for t in cols:
                    pe = max(pe, ready[s, t], done_at[t]) + PRODUCT
                    free.append((pe, slot_of[s, t]))
                vector.append((pe + 0.1, "add", len(products)))
                products.append((s, cols))
                if cols[-1] == NB - 1:
                    vector.append((pe + 3.0 + 2 * PRODUCT, "finish", s))
            todo.pop(0)

    read_of, act = [0] * NB, []
    for o in order:
        if o[0] in ("degree", "product"):
            continue
        kind, s, t = o
        assert free, "more tiles are kept than fit"
        freed, slot = min(free)
        free.remove((freed, slot))
        now = max(now, freed) + LOAD
        k = len(loads)
        loads.append((kind, s, t, slot))
        if kind != "again":
            read_of[s] += 1
            if read_of[s] == NB:
                last_first[s] = now
        if kind != "again":
            n = sum(how != "again" for how, *_ in loads)
            pool.append((now, "sum", k)) if n % 2 or s == t else act.append(k)
        if kind == "sum_only":
            free.append((now + SUMS, slot))
        else:
            wait = now + (0.2 if kind == "again" else SUMS)
            vector.append((wait, "turn", k))
            ready[s, t], slot_of[s, t] = wait + TURN, slot
        run_pe()
    assert not todo
    return loads, pe_steps, products, act, *([v[1:] for v in sorted(e, key=lambda v: v[0])] for e in (vector, pool))


def gcn_resnorm(nc: bass.Bass, x: bass.AP, adj: bass.AP, w: bass.AP, out: bass.AP):
    fp32 = mybir.dt.float32
    ALU = mybir.AluOpType
    ACT = mybir.ActivationFunctionType
    AX = mybir.AxisListType

    loads, pe_steps, products, on_act, vector_steps, pool_steps = plan()
    first_reads = [k for k, (kind, *_) in enumerate(loads) if kind != "again"]
    pool_nth = {k: n + 1 for n, k in enumerate(k for kind, k in pool_steps if kind == "sum")}
    act_nth = {k: n + 1 for n, k in enumerate(on_act)}
    turned = [k for kind, k in vector_steps if kind == "turn"]
    turn_nth = {k: n + 1 for n, k in enumerate(turned)}
    load_of = {(s, t): k for k, (kind, s, t, _) in enumerate(loads) if kind != "sum_only"}
    product_of = {(s, t): n for n, (s, cols) in enumerate(products) for t in cols}
    degree_nth = {r: n + 1 for n, r in enumerate(r for kind, r, *_ in pe_steps if kind == "degree")}
    finished = [s for s, cols in products if cols[-1] == NB - 1]
    final_of = {s: n for n, (s, cols) in enumerate(products) if cols[-1] == NB - 1}
    fill, fills = [], [0] * SLOTS
    before = []
    last_in = {}
    for k, (_, _, _, slot) in enumerate(loads):
        fills[slot] += 1
        fill.append(fills[slot])
        before.append(last_in.get(slot))
        last_in[slot] = k

    BANKS = 5

    with ExitStack() as ctx:
        def sb(name, shape):
            return ctx.enter_context(nc.sbuf_tensor(name, shape, fp32))

        def pb(name, shape):
            return ctx.enter_context(nc.psum_tensor(name, shape, fp32))

        def sem(name):
            return ctx.enter_context(nc.semaphore(name))

        tiles = [sb(f"tile{n}", [128, G, 128]) for n in range(SLOTS)]
        xs = sb("xs", [128, NB, CH, F])
        hT = sb("hT", [128, NB, CH, Q, 32])
        part = sb("part", [128, NB, G, NB])
        tree = sb("tree", [128, G, 64])
        rsum = sb("rsum", [128, 2, G])
        deg = sb("deg", [128, CH])
        power = sb("power", [128, CH])
        d = sb("d", [128, NB, CH])
        same = sb("same", [128, Q, 32])
        ident = sb("ident", [128, Q, 32])
        w_sb = sb("w_sb", [F, F])
        late = part[:, :, :, :].rearrange("p s g t -> p (s g t)").rearrange("p (n b f) -> p n b f", b=CH, f=F)
        res, pos, neg = late[:, 0:2], late[:, 2:5], late[:, 5:8]
        stats = sb("stats", [128, CH, 6])
        mv = sb("mv", [128, 3, CH, 2])
        neg_mean = sb("neg_mean", [128, CH])
        var_eps = sb("var_eps", [128, CH])
        rstd = sb("rstd", [128, 3, CH])
        shift = sb("shift", [128, 3, CH])

        p_prod = [pb(f"p_prod{n}", [128, B]) for n in range(BANKS)]
        p_deg = pb("p_deg", [128, B])
        p_out = [pb(f"p_out{n}", [128, CH, F]) for n in range(2)]

        x_loaded = [sem(f"x_loaded{n}") for n in range(3)]
        w_loaded = sem("w_loaded")
        loaded = [sem(f"loaded{n}") for n in range(SLOTS)]
        res_loaded = [sem(f"res_loaded{n}") for n in range(2)]
        cleared = sem("cleared")
        consts = sem("consts")
        act_summed = sem("act_summed")
        pool_summed = sem("pool_summed")
        pool_step = sem("pool_step")
        tile_turned = sem("tile_turned")
        row_summed = sem("row_summed")
        degree_out = sem("degree_out")
        deg_ready = sem("deg_ready")
        d_ready = sem("d_ready")
        var_ready = sem("var_ready")
        xs_ready = sem("xs_ready")
        product_out = sem("product_out")
        product_added = sem("product_added")
        hw_out = sem("hw_out")
        relu_neg = sem("relu_neg")
        exp_ready = sem("exp_ready")
        relu_pos = sem("relu_pos")
        z_ready = sem("z_ready")
        elu_ready = sem("elu_ready")
        y_ready = sem("y_ready")
        stats_ready = sem("stats_ready")
        mv_ready = sem("mv_ready")
        rstd_ready = sem("rstd_ready")
        norm_ready = sem("norm_ready")
        normed = sem("normed")
        stored = [sem(f"stored{n}") for n in range(3)]

        block = ctx.enter_context(nc.Block())

        adj_v = adj.rearrange("(s g i) (t q c) -> s t q i g c", g=G, i=32, q=Q, c=128)
        x_v = x.rearrange("(t q b j) f -> t q j b f", q=Q, b=CH, j=32)
        out_v = out.rearrange("(t q b j) f -> t q j b f", q=Q, b=CH, j=32)
        X_PARTS = [(0, 2), (2, 6), (6, NB)]
        x_part = {t: n for n, (a, b) in enumerate(X_PARTS) for t in range(a, b)}

        def quadrant(q):
            return slice(32 * q, 32 * q + 32)

        @block.sync
        def _(sp):
            def load_x(n):
                a, b = X_PARTS[n]
                for q in range(Q):
                    for t in range(a, b):
                        sp.dma_start(xs[quadrant(q), t], x_v[t, q]).then_inc(x_loaded[n], 16)

            sp.dma_start(w_sb[:, :], w).then_inc(w_loaded, 16)
            for k, (kind, s, t, slot) in enumerate(loads):
                if before[k] is not None:
                    was, s0, t0, _ = loads[before[k]]
                    if was == "sum_only":
                        if before[k] in act_nth:
                            sp.wait_ge(act_summed, act_nth[before[k]])
                        else:
                            sp.wait_ge(pool_summed, pool_nth[before[k]])
                    else:
                        sp.wait_ge(product_out, product_of[s0, t0] + 1)
                for q in range(Q):
                    sp.dma_start(tiles[slot][quadrant(q)], adj_v[s, t, q]).then_inc(loaded[slot], 16)
                for n, after in enumerate((NB - 3, 3 * NB, 8 * NB)):
                    if k == after:
                        load_x(n)

        @block.gpsimd
        def _(pool):
            nc.gpsimd.memset(same[:, :, :], 0.0).then_inc(cleared, 1)
            nc.gpsimd.memset(ident[:, :, :], 0.0).then_inc(cleared, 1)
            pool.wait_ge(cleared, 2)
            nc.gpsimd.affine_select(out=ident[:, :, :], in_=ident[:, :, :], compare_op=ALU.not_equal, fill=1.0,
                                    base=0, pattern=[[-32, Q], [-1, 32]], channel_multiplier=1).then_inc(consts, 1)
            for q in range(Q):
                if q:
                    pool.wait_ge(consts, q + 1)
                nc.gpsimd.affine_select(out=same[:, :, :], in_=same[:, :, :], compare_op=ALU.not_equal, fill=1.0,
                                        base=-32 * q, pattern=[[0, Q], [-1, 32]],
                                        channel_multiplier=1).then_inc(consts, 1)
            pool.wait_ge(consts, 1 + Q)
            nc.gpsimd.memset(power[:, :], -0.5).then_inc(consts, 1)
            pool.wait_ge(consts, 2 + Q)
            steps = 0
            for kind, k in pool_steps:
                if kind == "power":
                    r = k
                    pool.wait_ge(deg_ready, degree_nth[r])
                    nc.gpsimd.tensor_tensor(d[:, r], deg[:, :], power[:, :], ALU.pow).then_inc(d_ready, 1)
                    continue
                _, s, t, slot = loads[k]
                tile = tiles[slot]
                pool.wait_ge(loaded[slot], 64 * fill[k])
                if s == t:
                    diag = tile[:, :, :].rearrange("p (q b) c -> p b q c", q=Q)
                    for b in range(CH):
                        nc.gpsimd.tensor_tensor(diag[:, b, :, 32 * b:32 * b + 32], diag[:, b, :, 32 * b:32 * b + 32],
                                                ident[:, :, :], ALU.add).then_inc(pool_step, 1)
                    steps += CH
                    pool.wait_ge(pool_step, steps)
                if pool_nth[k] > 1:
                    pool.wait_ge(pool_summed, pool_nth[k] - 1)
                half = 64
                src = tile
                while half > 1:
                    nc.gpsimd.tensor_tensor(tree[:, :, 0:half], src[:, :, 0:half], src[:, :, half:2 * half],
                                            ALU.add).then_inc(pool_step, 1)
                    steps += 1
                    pool.wait_ge(pool_step, steps)
                    src = tree
                    half //= 2
                nc.gpsimd.tensor_tensor(part[:, s, :, t], tree[:, :, 0], tree[:, :, 1],
                                        ALU.add).then_inc(pool_summed, 1)
            def inverse_deviation(n):
                pool.wait_ge(mv_ready, n + 1)
                nc.gpsimd.tensor_scalar(var_eps[:, :], mv[:, n % 3, :, 1], EPS, None, ALU.add).then_inc(var_ready, 1)
                nc.gpsimd.tensor_scalar(neg_mean[:, :], mv[:, n % 3, :, 0], -1.0, None, ALU.mult).then_inc(var_ready, 1)
                pool.wait_ge(var_ready, 2 * n + 2)
                if n >= 3:
                    pool.wait_ge(normed, n - 2)
                nc.gpsimd.tensor_tensor(rstd[:, n % 3], var_eps[:, :], power[:, :], ALU.pow).then_inc(rstd_ready, 1)
                pool.wait_ge(rstd_ready, n + 1)
                nc.gpsimd.tensor_tensor(shift[:, n % 3], neg_mean[:, :], rstd[:, n % 3], ALU.mult)\
                  .then_inc(norm_ready, 1)
                pool.wait_ge(norm_ready, n + 1)

            def add_residual(n):
                pool.wait_ge(elu_ready, n + 1)
                pool.wait_ge(res_loaded[n % 2], 64 * (n // 2 + 1))
                nc.gpsimd.tensor_tensor(pos[:, n % 3], pos[:, n % 3], res[:, n % 2], ALU.add).then_inc(y_ready, 1)

            for n in range(NB):
                if n >= 1:
                    inverse_deviation(n - 1)
                add_residual(n)
            inverse_deviation(NB - 1)

        @block.scalar
        def _(act):
            for k in on_act:
                _, s, t, slot = loads[k]
                act.wait_ge(loaded[slot], 64 * fill[k])
                for g in range(G):
                    ins = nc.scalar.activation(tiles[slot][:, g], tiles[slot][:, g], ACT.Copy,
                                               accum_out=part[:, s, g, t:t + 1])
                ins.then_inc(act_summed, 1)

            def load_residual(n):
                for q in range(Q):
                    act.dma_start(res[quadrant(q), n % 2], x_v[finished[n], q]).then_inc(res_loaded[n % 2], 16)

            def store(n):
                s = finished[n]
                act.wait_ge(norm_ready, n + 1)
                if n + 2 < NB:
                    load_residual(n + 2)
                for b in range(CH):
                    ins = nc.scalar.activation(neg[:, n % 3, b], pos[:, n % 3, b], ACT.Identity,
                                               scale=rstd[:, n % 3, b:b + 1], bias=shift[:, n % 3, b:b + 1])
                ins.then_inc(normed, 1)
                act.wait_ge(normed, n + 1)
                for q in range(Q):
                    act.dma_start(out_v[s, q], neg[quadrant(q), n % 3]).then_inc(stored[n % 3], 16)

            act.wait_ge(row_summed, NB)
            load_residual(0)
            load_residual(1)
            for n in range(NB):
                if n >= 2:
                    store(n - 2)
                act.wait_ge(z_ready, n + 1)
                if n >= 3:
                    act.wait_ge(stored[n % 3], 64 * (n // 3))
                nc.scalar.activation(neg[:, n % 3], pos[:, n % 3], ACT.Relu, scale=-1.0).then_inc(relu_neg, 1)
                act.wait_ge(relu_neg, n + 1)
                nc.scalar.activation(pos[:, n % 3], pos[:, n % 3], ACT.Relu).then_inc(relu_pos, 1)
                nc.scalar.activation(neg[:, n % 3], neg[:, n % 3], ACT.Exp, scale=-1.0).then_inc(exp_ready, 1)
            store(NB - 2)
            store(NB - 1)
            for n in range(3):
                act.wait_ge(stored[n], 64 * len(range(n, NB, 3)))

        @block.tensor
        def _(pe):
            def out_rows(n):
                s = finished[n]
                if n >= 2:
                    pe.wait_ge(z_ready, n - 1)
                for b in range(CH):
                    ins = nc.tensor.matmul(p_out[n % 2][:, b], hT[:, s, b], w_sb[:, :], start=True, stop=True)
                ins.then_inc(hw_out, 1)

            pe.wait_ge(consts, 2 + Q)
            pe.wait_ge(w_loaded, 16)
            nth = 0
            finals = 0
            for kind, s, *rest in pe_steps:
                if kind == "degree":
                    pe.wait_ge(row_summed, degree_nth[s])
                    if degree_nth[s] > 1:
                        pe.wait_ge(deg_ready, degree_nth[s] - 1)
                    for q in range(Q):
                        ins = nc.tensor.matmul(p_deg[quadrant(q), 0:CH], same[:, q], rsum[:, degree_nth[s] % 2, CH * q:CH * q + CH],
                                               start=True, stop=True)
                    ins.then_inc(degree_out, 1)
                    continue
                cols = rest[0]
                if nth >= BANKS:
                    pe.wait_ge(product_added, nth - BANKS + 1)
                for t in cols:
                    pe.wait_ge(xs_ready, degree_nth[t])
                    pe.wait_ge(tile_turned, turn_nth[load_of[s, t]])
                    tile = tiles[loads[load_of[s, t]][3]]
                    chunks = tile[:, :, :].rearrange("p g (b i) -> p b g i", b=CH)
                    for b in range(CH):
                        ins = nc.tensor.matmul(p_prod[nth % BANKS][:, :].rearrange("f (g i) -> f g i", g=G),
                                               xs[:, t, b], chunks[:, b],
                                               start=(t == cols[0] and b == 0), stop=(t == cols[-1] and b == CH - 1))
                ins.then_inc(product_out, 1)
                nth += 1
                if cols[-1] == NB - 1:
                    finals += 1
                    if finals >= 3:
                        pe.wait_ge(product_added, final_of[finished[finals - 3]] + 1)
                        out_rows(finals - 3)
            for n in (NB - 2, NB - 1):
                pe.wait_ge(product_added, final_of[finished[n]] + 1)
                out_rows(n)

        @block.vector
        def _(dve):
            def scale_rows(n):
                s = finished[n]
                dve.wait_ge(hw_out, n + 1)
                if n >= 3:
                    dve.wait_ge(normed, n - 2)
                for b in range(CH):
                    ins = nc.vector.tensor_scalar(pos[:, n % 3, b], p_out[n % 2][:, b], d[:, s, b:b + 1], None, ALU.mult)
                ins.then_inc(z_ready, 1)

            def elu(n):
                dve.wait_ge(relu_pos, n + 1)
                dve.wait_ge(exp_ready, n + 1)
                nc.vector.scalar_tensor_tensor(out=pos[:, n % 3], in0=neg[:, n % 3], scalar=-1.0, in1=pos[:, n % 3],
                                               op0=ALU.add, op1=ALU.add).then_inc(elu_ready, 1)

            def norm(n):
                dve.wait_ge(y_ready, n + 1)
                if n >= 3:
                    dve.wait_ge(norm_ready, n - 2)
                for b in range(CH):
                    ins = nc.vector.bn_stats(stats[:, b], pos[:, n % 3, b])
                ins.then_inc(stats_ready, 1)
                dve.wait_ge(stats_ready, n + 1)
                for b in range(CH):
                    ins = nc.vector.bn_aggr(mv[:, n % 3, b], stats[:, b])
                ins.then_inc(mv_ready, 1)

            finish_nth = 0
            for kind, arg in vector_steps:
                if kind == "turn":
                    k = arg
                    how, s, t, slot = loads[k]
                    if how == "again":
                        dve.wait_ge(loaded[slot], 64 * fill[k])
                    elif k in act_nth:
                        dve.wait_ge(act_summed, act_nth[k])
                    else:
                        dve.wait_ge(pool_summed, pool_nth[k])
                    nc.vector.transpose(tiles[slot][:, :, :], tiles[slot][:, :, :]).then_inc(tile_turned, 1)
                elif kind == "row_sum":
                    r = arg
                    in_row = [k for k in first_reads if loads[k][1] == r]
                    acts = [act_nth[k] for k in in_row if k in act_nth]
                    pools = [pool_nth[k] for k in in_row if k in pool_nth]
                    dve.wait_ge(act_summed, max(acts))
                    dve.wait_ge(pool_summed, max(pools))
                    if degree_nth[r] > 2:
                        dve.wait_ge(degree_out, degree_nth[r] - 2)
                    nc.vector.tensor_reduce(rsum[:, degree_nth[r] % 2], part[:, r], AX.X, ALU.add).then_inc(row_summed, 1)
                elif kind == "degree":
                    r = arg
                    nth = degree_nth[r]
                    dve.wait_ge(degree_out, nth)
                    if nth > 1:
                        dve.wait_ge(d_ready, nth - 1)
                    nc.vector.tensor_copy(deg[:, :], p_deg[:, 0:CH]).then_inc(deg_ready, 1)
                elif kind == "scale":
                    r = arg
                    nth = degree_nth[r]
                    dve.wait_ge(d_ready, nth)
                    a, b = X_PARTS[x_part[r]]
                    dve.wait_ge(x_loaded[x_part[r]], 16 * Q * (b - a))
                    for b in range(CH):
                        ins = nc.vector.tensor_scalar(xs[:, r, b], xs[:, r, b], d[:, r, b:b + 1], None, ALU.mult)
                    ins.then_inc(xs_ready, 1)
                elif kind == "add":
                    n = arg
                    s, cols = products[n]
                    dve.wait_ge(product_out, n + 1)
                    rows = hT[:, s].rearrange("f b q i -> f q b i")
                    product = p_prod[n % BANKS][:, :].rearrange("f (q b i) -> f q b i", q=Q, b=CH)
                    if cols[0] == 0:
                        nc.vector.tensor_copy(rows, product).then_inc(product_added, 1)
                    else:
                        nc.vector.tensor_tensor(rows, product, rows, ALU.add).then_inc(product_added, 1)
                else:
                    if finish_nth >= 2:
                        norm(finish_nth - 2)
                    scale_rows(finish_nth)
                    if finish_nth >= 1:
                        elu(finish_nth - 1)
                    finish_nth += 1
            norm(NB - 2)
            elu(NB - 1)
            norm(NB - 1)


def kernel(x, adj, L0_gnn_w):
    import numpy as _np
    import concourse.bacc as _bacc
    from concourse import mybir as _mybir
    from concourse.bass_utils import run_bass_kernel_spmd as _run

    nc = _bacc.Bacc("TRN2", target_bir_lowering=False, num_devices=1)
    arrays, args = {}, []
    for name, a in (("x", x), ("adj", adj), ("w", L0_gnn_w)):
        a = _np.ascontiguousarray(a)
        arrays[f"in_{name}"] = a
        args.append(nc.dram_tensor(f"in_{name}", a.shape, _mybir.dt.from_np(a.dtype), kind="ExternalInput").ap())
    args.append(nc.dram_tensor("out_rows", (N, F), _mybir.dt.float32, kind="ExternalOutput").ap())
    gcn_resnorm(nc, *args)
    return _run(nc, [arrays], core_ids=[0]).results[0]["out_rows"]
```

```python
import concourse.bass as bass
from concourse import mybir
from contextlib import ExitStack

N = 8192
F = 128
NB = 16
B = N // NB
G = B // 32
Q = 4
CH = B // 128
SLOTS = 18
KEEP = 6
COLUMNS = [[n] for n in range(NB - 2)] + [[NB - 2, NB - 1]]
POOL_OF = (1, 2)
AHEAD = 8.0
LEAD = 1
EPS = 1e-5


def plan():
    LOAD, PRODUCT, SUMS, TURN = 2.93, 3.42, 5.0, 2.2
    order, pe_steps, kept, read = [], [], set(), set()

    def read_rows(cols):
        for r in cols:
            inside = [t for t in cols if (r, t) not in read]
            later = list(range(cols[-1] + 1, NB))
            room = max(0, KEEP - sum(t > cols[-1] for _, t in kept))
            order.extend(("sum_only", r, t) for t in reversed(later[room:]))
            order.extend(("keep", r, t) for t in reversed(later[:room]))
            order.extend(("keep", r, t) for t in inside)
            kept.update((r, t) for t in inside + later[:room])
            read.update((r, t) for t in inside + later)
            pe_steps.append(("degree", r))

    def multiply(rows, cols):
        for s in rows:
            for t in cols:
                if (s, t) not in kept:
                    order.append(("again" if (s, t) in read else "stream", s, t))
                    read.add((s, t))
            pe_steps.append(("product", s, cols))

    read_rows(COLUMNS[0])
    for n, cols in enumerate(COLUMNS):
        rows = [s for s in range(NB) if all((s, t) in kept for t in cols)]
        rows += [s for s in range(cols[-1] + 1, NB)]
        fresh = len(rows)
        rows += [s for s in range(NB) if s not in rows]
        if n + 1 == len(COLUMNS):
            multiply(rows, cols)
        else:
            at = min(fresh, NB - LEAD)
            multiply(rows[:at], cols)
            held_back = len(pe_steps)
            multiply(rows[at:fresh], cols)
            read_rows(COLUMNS[n + 1])
            degrees = [step for step in pe_steps if step[0] == "degree" and step[1] in COLUMNS[n + 1]]
            pe_steps[:] = [step for step in pe_steps if step not in degrees]
            pe_steps[held_back:held_back] = degrees
            multiply(rows[fresh:], cols)
        kept -= {(s, t) for s, t in kept if t <= cols[-1]}
    assert len(read) == NB * NB

    loads = []
    free = [(0.0, n) for n in range(SLOTS)]
    now, pe, last_first = 0.0, 0.0, {}
    ready, slot_of, load_at = {}, {}, {}
    todo = list(pe_steps)
    vector, pool, products, done_at = [], [], [], {}

    def run_pe():
        nonlocal pe
        while todo:
            step = todo[0]
            if step[0] == "degree":
                if step[1] not in last_first:
                    return
                t0 = last_first[step[1]] + SUMS
                if step[1] - 1 in col_read:
                    vector.append((max(col_read.pop(step[1] - 1) + SUMS, t0 - 1.5), "column_sum", step[1] - 1))
                vector.append((t0, "row_sum", step[1]))
                pe = max(pe, t0 + 0.5) + 0.3
                vector.append((pe + 0.1, "degree", step[1]))
                pool.append((pe + 0.5, "power", step[1]))
                vector.append((pe + 1.0, "scale", step[1]))
                done_at[step[1]] = pe + 2.5
            else:
                _, s, cols = step
                if any((s, t) not in ready for t in cols) or any(t not in done_at for t in cols):
                    return
                for t in cols:
                    pe = max(pe, ready[s, t], done_at[t])
                    vector.append((max(ready[s, t], pe - AHEAD) - TURN, "turn", load_at[s, t]))
                    pe += PRODUCT
                    free.append((pe, slot_of[s, t]))
                vector.append((pe + 0.1, "add", len(products)))
                products.append((s, cols))
                if cols[-1] == NB - 1:
                    vector.append((pe + 3.0 + 2 * PRODUCT, "finish", s))
            todo.pop(0)

    read_of, act, col_read = [0] * NB, [], {}
    for kind, s, t in order:
        assert free, "more tiles are kept than fit"
        freed, slot = min(free)
        free.remove((freed, slot))
        now = max(now, freed) + LOAD
        k = len(loads)
        loads.append((kind, s, t, slot))
        if kind == "stream":
            col_read[t] = now
        if kind != "again":
            read_of[s] += 1
            if read_of[s] == NB:
                last_first[s] = now
        if kind != "again":
            n = sum(how != "again" for how, *_ in loads)
            if n % POOL_OF[1] < POOL_OF[0] or s == t:
                pool.append((now, "sum", k))
                vector.append((now + 3.9, "quarters", k))
            else:
                act.append(k)
        if kind == "sum_only":
            free.append((now + SUMS, slot))
        else:
            wait = now + (0.2 if kind == "again" else SUMS)
            ready[s, t], slot_of[s, t], load_at[s, t] = wait + TURN, slot, k
        run_pe()
    assert not todo
    return loads, pe_steps, products, act, *([v[1:] for v in sorted(e, key=lambda v: v[0])] for e in (vector, pool))


def gcn_resnorm(nc: bass.Bass, x: bass.AP, adj: bass.AP, w: bass.AP, out: bass.AP):
    fp32 = mybir.dt.float32
    ALU = mybir.AluOpType
    ACT = mybir.ActivationFunctionType
    AX = mybir.AxisListType

    loads, pe_steps, products, on_act, vector_steps, pool_steps = plan()
    first_reads = [k for k, (kind, *_) in enumerate(loads) if kind != "again"]
    first_col = {t: cols[0] for cols in COLUMNS for t in cols}
    with_row = {k for k in first_reads if loads[k][2] >= first_col[loads[k][1]]}
    last_read = {s: k for k, (kind, s, *_) in enumerate(loads) if kind != "again"}
    x_after = {k - 3: s for s, k in last_read.items()}
    pool_nth = {k: n + 1 for n, k in enumerate(k for kind, k in pool_steps if kind == "sum")}
    act_nth = {k: n + 1 for n, k in enumerate(on_act)}
    turned = [k for kind, k in vector_steps if kind == "turn"]
    turn_nth = {k: n + 1 for n, k in enumerate(turned)}
    load_of = {(s, t): k for k, (kind, s, t, _) in enumerate(loads) if kind != "sum_only"}
    product_of = {(s, t): n for n, (s, cols) in enumerate(products) for t in cols}
    degree_nth = {r: n + 1 for n, r in enumerate(r for kind, r, *_ in pe_steps if kind == "degree")}
    finished = [s for s, cols in products if cols[-1] == NB - 1]
    final_of = {s: n for n, (s, cols) in enumerate(products) if cols[-1] == NB - 1}
    fill, fills = [], [0] * SLOTS
    before = []
    last_in = {}
    for k, (_, _, _, slot) in enumerate(loads):
        fills[slot] += 1
        fill.append(fills[slot])
        before.append(last_in.get(slot))
        last_in[slot] = k

    BANKS = 5

    with ExitStack() as ctx:
        def sb(name, shape):
            return ctx.enter_context(nc.sbuf_tensor(name, shape, fp32))

        def pb(name, shape):
            return ctx.enter_context(nc.psum_tensor(name, shape, fp32))

        def sem(name):
            return ctx.enter_context(nc.semaphore(name))

        tiles = [sb(f"tile{n}", [128, G, 128]) for n in range(SLOTS)]
        xs = sb("xs", [128, NB, CH, F])
        hT = sb("hT", [128, NB, CH, Q, 32])
        row_part = sb("row_part", [128, 2, NB, G])
        col_part = sb("col_part", [128, 2, NB, G])
        sums = sb("sums", [128, NB, G])
        halves = sb("halves", [128, G, 64])
        quarters = sb("quarters", [128, 2, G, 32])
        rsum = sb("rsum", [128, 2, G])
        deg = sb("deg", [128, CH])
        power = sb("power", [128, CH])
        d = sb("d", [128, NB, CH])
        same = sb("same", [128, Q, 32])
        ident = sb("ident", [128, Q, 32])
        w_sb = sb("w_sb", [F, F])
        res, pos, neg = xs[:, 0:2], xs[:, 2:5], xs[:, 5:8]
        stats = sb("stats", [128, CH, 6])
        mv = sb("mv", [128, 3, CH, 2])
        neg_mean = sb("neg_mean", [128, CH])
        var_eps = sb("var_eps", [128, CH])
        rstd = sb("rstd", [128, 3, CH])
        shift = sb("shift", [128, 3, CH])

        p_prod = [pb(f"p_prod{n}", [128, B]) for n in range(BANKS)]
        p_deg = pb("p_deg", [128, B])
        p_out = [pb(f"p_out{n}", [128, CH, F]) for n in range(2)]

        x_loaded = [sem(f"x_loaded{n}") for n in range(2)]
        w_loaded = sem("w_loaded")
        loaded = [sem(f"loaded{n}") for n in range(SLOTS)]
        res_loaded = [sem(f"res_loaded{n}") for n in range(2)]
        cleared = sem("cleared")
        consts = sem("consts")
        act_summed = sem("act_summed")
        pool_summed = sem("pool_summed")
        pool_step = sem("pool_step")
        pool_halved = sem("pool_halved")
        quarters_summed = sem("quarters_summed")
        tile_turned = sem("tile_turned")
        row_read = sem("row_read")
        row_summed = sem("row_summed")
        col_summed = sem("col_summed")
        degree_out = sem("degree_out")
        deg_ready = sem("deg_ready")
        d_ready = sem("d_ready")
        var_ready = sem("var_ready")
        xs_ready = sem("xs_ready")
        product_out = sem("product_out")
        product_added = sem("product_added")
        hw_out = sem("hw_out")
        relu_neg = sem("relu_neg")
        exp_ready = sem("exp_ready")
        relu_pos = sem("relu_pos")
        z_ready = sem("z_ready")
        elu_ready = sem("elu_ready")
        y_ready = sem("y_ready")
        stats_ready = sem("stats_ready")
        mv_ready = sem("mv_ready")
        rstd_ready = sem("rstd_ready")
        norm_ready = sem("norm_ready")
        normed = sem("normed")
        stored = [sem(f"stored{n}") for n in range(3)]

        block = ctx.enter_context(nc.Block())

        adj_v = adj.rearrange("(s g i) (t q c) -> s t q i g c", g=G, i=32, q=Q, c=128)
        x_v = x.rearrange("(t q b j) f -> t q j b f", q=Q, b=CH, j=32)
        out_v = out.rearrange("(t q b j) f -> t q j b f", q=Q, b=CH, j=32)

        def quadrant(q):
            return slice(32 * q, 32 * q + 32)

        def sum_at(k):
            _, s, t, _ = loads[k]
            return row_part[:, s % 2, t] if k in with_row else col_part[:, t % 2, s]

        def wait_sum_free(engine, k):
            _, s, t, _ = loads[k]
            if k in with_row and s >= 2:
                engine.wait_ge(row_summed, s - 1)
            if k not in with_row and t >= 2:
                engine.wait_ge(col_summed, t - 1)

        @block.sync
        def _(sp):
            sp.dma_start(w_sb[:, :], w).then_inc(w_loaded, 16)
            for k, (kind, s, t, slot) in enumerate(loads):
                if before[k] is not None:
                    was, s0, t0, _ = loads[before[k]]
                    if was == "sum_only":
                        if before[k] in act_nth:
                            sp.wait_ge(act_summed, act_nth[before[k]])
                        else:
                            sp.wait_ge(pool_summed, pool_nth[before[k]])
                    else:
                        sp.wait_ge(product_out, product_of[s0, t0] + 1)
                for q in range(Q):
                    sp.dma_start(tiles[slot][quadrant(q)], adj_v[s, t, q]).then_inc(loaded[slot], 16)
                if k in x_after:
                    r = x_after[k]
                    if r >= 2:
                        sp.wait_ge(xs_ready, r - 1)
                    for q in range(Q):
                        sp.dma_start(xs[quadrant(q), r], x_v[r, q]).then_inc(x_loaded[r % 2], 16)

        @block.gpsimd
        def _(pool):
            nc.gpsimd.memset(same[:, :, :], 0.0).then_inc(cleared, 1)
            nc.gpsimd.memset(ident[:, :, :], 0.0).then_inc(cleared, 1)
            pool.wait_ge(cleared, 2)
            nc.gpsimd.affine_select(out=ident[:, :, :], in_=ident[:, :, :], compare_op=ALU.not_equal, fill=1.0,
                                    base=0, pattern=[[-32, Q], [-1, 32]], channel_multiplier=1).then_inc(consts, 1)
            for q in range(Q):
                if q:
                    pool.wait_ge(consts, q + 1)
                nc.gpsimd.affine_select(out=same[:, :, :], in_=same[:, :, :], compare_op=ALU.not_equal, fill=1.0,
                                        base=-32 * q, pattern=[[0, Q], [-1, 32]],
                                        channel_multiplier=1).then_inc(consts, 1)
            pool.wait_ge(consts, 1 + Q)
            nc.gpsimd.memset(power[:, :], -0.5).then_inc(consts, 1)
            pool.wait_ge(consts, 2 + Q)
            steps = 0
            for kind, k in pool_steps:
                if kind == "power":
                    r = k
                    pool.wait_ge(deg_ready, degree_nth[r])
                    nc.gpsimd.tensor_tensor(d[:, r], deg[:, :], power[:, :], ALU.pow).then_inc(d_ready, 1)
                    continue
                _, s, t, slot = loads[k]
                tile = tiles[slot]
                pool.wait_ge(loaded[slot], 64 * fill[k])
                if s == t:
                    diag = tile[:, :, :].rearrange("p (q b) c -> p b q c", q=Q)
                    for b in range(CH):
                        nc.gpsimd.tensor_tensor(diag[:, b, :, 32 * b:32 * b + 32], diag[:, b, :, 32 * b:32 * b + 32],
                                                ident[:, :, :], ALU.add).then_inc(pool_step, 1)
                    steps += CH
                    pool.wait_ge(pool_step, steps)
                if pool_nth[k] > 1:
                    pool.wait_ge(pool_summed, pool_nth[k] - 1)
                nth = pool_nth[k]
                nc.gpsimd.tensor_tensor(halves[:, :, :], tile[:, :, 0:64], tile[:, :, 64:128], ALU.add)\
                  .then_inc(pool_halved, 1)
                pool.wait_ge(pool_halved, nth)
                if nth > 2:
                    pool.wait_ge(quarters_summed, nth - 2)
                nc.gpsimd.tensor_tensor(quarters[:, nth % 2], halves[:, :, 0:32], halves[:, :, 32:64], ALU.add)\
                  .then_inc(pool_summed, 1)
            def inverse_deviation(n):
                pool.wait_ge(mv_ready, n + 1)
                nc.gpsimd.tensor_scalar(var_eps[:, :], mv[:, n % 3, :, 1], EPS, None, ALU.add).then_inc(var_ready, 1)
                nc.gpsimd.tensor_scalar(neg_mean[:, :], mv[:, n % 3, :, 0], -1.0, None, ALU.mult).then_inc(var_ready, 1)
                pool.wait_ge(var_ready, 2 * n + 2)
                if n >= 3:
                    pool.wait_ge(normed, n - 2)
                nc.gpsimd.tensor_tensor(rstd[:, n % 3], var_eps[:, :], power[:, :], ALU.pow).then_inc(rstd_ready, 1)
                pool.wait_ge(rstd_ready, n + 1)
                nc.gpsimd.tensor_tensor(shift[:, n % 3], neg_mean[:, :], rstd[:, n % 3], ALU.mult)\
                  .then_inc(norm_ready, 1)
                pool.wait_ge(norm_ready, n + 1)

            def add_residual(n):
                pool.wait_ge(elu_ready, n + 1)
                pool.wait_ge(res_loaded[n % 2], 64 * (n // 2 + 1))
                nc.gpsimd.tensor_tensor(pos[:, n % 3], pos[:, n % 3], res[:, n % 2], ALU.add).then_inc(y_ready, 1)

            for n in range(NB):
                if n >= 1:
                    inverse_deviation(n - 1)
                add_residual(n)
            inverse_deviation(NB - 1)

        @block.scalar
        def _(act):
            for k in on_act:
                _, s, t, slot = loads[k]
                act.wait_ge(loaded[slot], 64 * fill[k])
                wait_sum_free(act, k)
                for g in range(G):
                    ins = nc.scalar.activation(tiles[slot][:, g], tiles[slot][:, g], ACT.Copy,
                                               accum_out=sum_at(k)[:, g:g + 1])
                ins.then_inc(act_summed, 1)

            def load_residual(n):
                for q in range(Q):
                    act.dma_start(res[quadrant(q), n % 2], x_v[finished[n], q]).then_inc(res_loaded[n % 2], 16)

            def store(n):
                s = finished[n]
                act.wait_ge(norm_ready, n + 1)
                if n + 2 < NB:
                    load_residual(n + 2)
                for b in range(CH):
                    ins = nc.scalar.activation(neg[:, n % 3, b], pos[:, n % 3, b], ACT.Identity,
                                               scale=rstd[:, n % 3, b:b + 1], bias=shift[:, n % 3, b:b + 1])
                ins.then_inc(normed, 1)
                act.wait_ge(normed, n + 1)
                for q in range(Q):
                    act.dma_start(out_v[s, q], neg[quadrant(q), n % 3]).then_inc(stored[n % 3], 16)

            act.wait_ge(product_out, final_of[finished[0]])
            load_residual(0)
            load_residual(1)
            for n in range(NB):
                if n >= 2:
                    store(n - 2)
                act.wait_ge(z_ready, n + 1)
                if n >= 3:
                    act.wait_ge(stored[n % 3], 64 * (n // 3))
                nc.scalar.activation(neg[:, n % 3], pos[:, n % 3], ACT.Relu, scale=-1.0).then_inc(relu_neg, 1)
                act.wait_ge(relu_neg, n + 1)
                nc.scalar.activation(pos[:, n % 3], pos[:, n % 3], ACT.Relu).then_inc(relu_pos, 1)
                nc.scalar.activation(neg[:, n % 3], neg[:, n % 3], ACT.Exp, scale=-1.0).then_inc(exp_ready, 1)
            store(NB - 2)
            store(NB - 1)
            for n in range(3):
                act.wait_ge(stored[n], 64 * len(range(n, NB, 3)))

        @block.tensor
        def _(pe):
            def out_rows(n):
                s = finished[n]
                if n >= 2:
                    pe.wait_ge(z_ready, n - 1)
                for b in range(CH):
                    ins = nc.tensor.matmul(p_out[n % 2][:, b], hT[:, s, b], w_sb[:, :], start=True, stop=True)
                ins.then_inc(hw_out, 1)

            pe.wait_ge(consts, 2 + Q)
            pe.wait_ge(w_loaded, 16)
            nth = 0
            finals = 0
            for kind, s, *rest in pe_steps:
                if kind == "degree":
                    pe.wait_ge(row_summed, degree_nth[s])
                    if degree_nth[s] > 1:
                        pe.wait_ge(deg_ready, degree_nth[s] - 1)
                    for q in range(Q):
                        ins = nc.tensor.matmul(p_deg[quadrant(q), 0:CH], same[:, q], rsum[:, degree_nth[s] % 2, CH * q:CH * q + CH],
                                               start=True, stop=True)
                    ins.then_inc(degree_out, 1)
                    continue
                cols = rest[0]
                if nth >= BANKS:
                    pe.wait_ge(product_added, nth - BANKS + 1)
                for t in cols:
                    pe.wait_ge(xs_ready, degree_nth[t])
                    pe.wait_ge(tile_turned, turn_nth[load_of[s, t]])
                    tile = tiles[loads[load_of[s, t]][3]]
                    chunks = tile[:, :, :].rearrange("p g (b i) -> p b g i", b=CH)
                    for b in range(CH):
                        ins = nc.tensor.matmul(p_prod[nth % BANKS][:, :].rearrange("f (g i) -> f g i", g=G),
                                               xs[:, t, b], chunks[:, b],
                                               start=(t == cols[0] and b == 0), stop=(t == cols[-1] and b == CH - 1))
                ins.then_inc(product_out, 1)
                nth += 1
                if cols[-1] == NB - 1:
                    finals += 1
                    if finals >= 3:
                        pe.wait_ge(product_added, final_of[finished[finals - 3]] + 1)
                        out_rows(finals - 3)
            for n in (NB - 2, NB - 1):
                pe.wait_ge(product_added, final_of[finished[n]] + 1)
                out_rows(n)

        @block.vector
        def _(dve):
            def scale_rows(n):
                s = finished[n]
                dve.wait_ge(hw_out, n + 1)
                if n >= 3:
                    dve.wait_ge(normed, n - 2)
                for b in range(CH):
                    ins = nc.vector.tensor_scalar(pos[:, n % 3, b], p_out[n % 2][:, b], d[:, s, b:b + 1], None, ALU.mult)
                ins.then_inc(z_ready, 1)

            def elu(n):
                dve.wait_ge(relu_pos, n + 1)
                dve.wait_ge(exp_ready, n + 1)
                nc.vector.scalar_tensor_tensor(out=pos[:, n % 3], in0=neg[:, n % 3], scalar=-1.0, in1=pos[:, n % 3],
                                               op0=ALU.add, op1=ALU.add).then_inc(elu_ready, 1)

            def norm(n):
                dve.wait_ge(y_ready, n + 1)
                if n >= 3:
                    dve.wait_ge(norm_ready, n - 2)
                for b in range(CH):
                    ins = nc.vector.bn_stats(stats[:, b], pos[:, n % 3, b])
                ins.then_inc(stats_ready, 1)
                dve.wait_ge(stats_ready, n + 1)
                for b in range(CH):
                    ins = nc.vector.bn_aggr(mv[:, n % 3, b], stats[:, b])
                ins.then_inc(mv_ready, 1)

            def wait_sums(dve, ks):
                if any(k in act_nth for k in ks):
                    dve.wait_ge(act_summed, max(act_nth[k] for k in ks if k in act_nth))
                if any(k in pool_nth for k in ks):
                    dve.wait_ge(quarters_summed, max(pool_nth[k] for k in ks if k in pool_nth))

            finish_nth = 0
            for kind, arg in vector_steps:
                if kind == "turn":
                    k = arg
                    how, s, t, slot = loads[k]
                    if how == "again":
                        dve.wait_ge(loaded[slot], 64 * fill[k])
                    elif k in act_nth:
                        dve.wait_ge(act_summed, act_nth[k])
                    else:
                        dve.wait_ge(pool_summed, pool_nth[k])
                    nc.vector.transpose(tiles[slot][:, :, :], tiles[slot][:, :, :]).then_inc(tile_turned, 1)
                elif kind == "quarters":
                    _, s, t, _ = loads[arg]
                    dve.wait_ge(pool_summed, pool_nth[arg])
                    wait_sum_free(dve, arg)
                    nc.vector.tensor_reduce(sum_at(arg), quarters[:, pool_nth[arg] % 2], AX.X, ALU.add)\
                      .then_inc(quarters_summed, 1)
                elif kind == "row_sum":
                    r = arg
                    nth = degree_nth[r]
                    wait_sums(dve, [k for k in with_row if loads[k][1] == r])
                    if nth > 2:
                        dve.wait_ge(degree_out, nth - 2)
                    own = row_part[:, r % 2, first_col[r]:].rearrange("p t g -> p g t")
                    ins = nc.vector.tensor_reduce(rsum[:, nth % 2], own, AX.X, ALU.add)
                    if r > 0:
                        ins.then_inc(row_read, 1)
                        dve.wait_ge(row_read, r)
                        ins = nc.vector.tensor_tensor(rsum[:, nth % 2], rsum[:, nth % 2], sums[:, r], ALU.add)
                    ins.then_inc(row_summed, 1)
                elif kind == "column_sum":
                    t = arg
                    wait_sums(dve, [k for k in first_reads if k not in with_row and loads[k][2] == t])
                    if t == 0:
                        nc.vector.tensor_copy(sums[:, 1:], col_part[:, 0, 1:]).then_inc(col_summed, 1)
                    else:
                        dve.wait_ge(col_summed, t)
                        nc.vector.tensor_tensor(sums[:, t + 1:], sums[:, t + 1:], col_part[:, t % 2, t + 1:], ALU.add)\
                          .then_inc(col_summed, 1)
                elif kind == "degree":
                    r = arg
                    nth = degree_nth[r]
                    dve.wait_ge(degree_out, nth)
                    if nth > 1:
                        dve.wait_ge(d_ready, nth - 1)
                    nc.vector.tensor_copy(deg[:, :], p_deg[:, 0:CH]).then_inc(deg_ready, 1)
                elif kind == "scale":
                    r = arg
                    nth = degree_nth[r]
                    dve.wait_ge(d_ready, nth)
                    dve.wait_ge(x_loaded[r % 2], 16 * Q * (r // 2 + 1))
                    for b in range(CH):
                        ins = nc.vector.tensor_scalar(xs[:, r, b], xs[:, r, b], d[:, r, b:b + 1], None, ALU.mult)
                    ins.then_inc(xs_ready, 1)
                elif kind == "add":
                    n = arg
                    s, cols = products[n]
                    dve.wait_ge(product_out, n + 1)
                    rows = hT[:, s].rearrange("f b q i -> f q b i")
                    product = p_prod[n % BANKS][:, :].rearrange("f (q b i) -> f q b i", q=Q, b=CH)
                    if cols[0] == 0:
                        nc.vector.tensor_copy(rows, product).then_inc(product_added, 1)
                    else:
                        nc.vector.tensor_tensor(rows, product, rows, ALU.add).then_inc(product_added, 1)
                else:
                    if finish_nth >= 2:
                        norm(finish_nth - 2)
                    scale_rows(finish_nth)
                    if finish_nth >= 1:
                        elu(finish_nth - 1)
                    finish_nth += 1
            norm(NB - 2)
            elu(NB - 1)
            norm(NB - 1)


def kernel(x, adj, L0_gnn_w):
    import numpy as _np
    import concourse.bacc as _bacc
    from concourse import mybir as _mybir
    from concourse.bass_utils import run_bass_kernel_spmd as _run

    nc = _bacc.Bacc("TRN2", target_bir_lowering=False, num_devices=1, dynamic_dma_scratch_size=256)
    arrays, args = {}, []
    for name, a in (("x", x), ("adj", adj), ("w", L0_gnn_w)):
        a = _np.ascontiguousarray(a)
        arrays[f"in_{name}"] = a
        args.append(nc.dram_tensor(f"in_{name}", a.shape, _mybir.dt.from_np(a.dtype), kind="ExternalInput").ap())
    args.append(nc.dram_tensor("out_rows", (N, F), _mybir.dt.float32, kind="ExternalOutput").ap())
    gcn_resnorm(nc, *args)
    return _run(nc, [arrays], core_ids=[0]).results[0]["out_rows"]
```

```python
import concourse.bass as bass
from concourse import mybir
from contextlib import ExitStack

N = 8192
F = 128
NB = 16
B = N // NB
G = B // 32
Q = 4
CH = B // 128
SLOTS = 20
LATE = 3
XRING = 4
KEEP = [7, 8, 8, 8, 8, 8, 8, 8, 8, 8, 7, 8, 8, 3, 8, 8]
COLUMNS = [[n] for n in range(NB - 2)] + [[NB - 2, NB - 1]]
POOL_OF = (2, 5)
LAG = 1
FINISH = 11.0
AHEAD = 5.8
LEAD = 1
EPS = 1e-5


def plan():
    LOAD, PRODUCT, SUMS, TURN = 2.91, 3.50, 4.2, 5.2
    order, pe_steps, kept, read = [], [], set(), set()
    first_col = {t: cols[0] for cols in COLUMNS for t in cols}

    def read_rows(cols):
        for r in cols:
            inside = [t for t in cols if (r, t) not in read]
            later = list(range(cols[-1] + 1, NB))
            room = max(0, KEEP[r] - sum(t > cols[-1] for _, t in kept))
            order.extend(("sum_only", r, t) for t in reversed(later[room:]))
            order.extend(("keep", r, t) for t in reversed(later[:room]))
            order.extend(("keep", r, t) for t in inside)
            kept.update((r, t) for t in inside + later[:room])
            read.update((r, t) for t in inside + later)
            pe_steps.append(("degree", r))

    def multiply(rows, cols):
        for s in rows:
            for t in cols:
                if (s, t) not in kept:
                    order.append(("again" if (s, t) in read else "stream", s, t))
                    read.add((s, t))
            pe_steps.append(("product", s, cols))

    read_rows(COLUMNS[0])
    for n, cols in enumerate(COLUMNS):
        rows = [s for s in range(NB) if all((s, t) in kept for t in cols)]
        rows += [s for s in range(cols[-1] + 1, NB)]
        fresh = len(rows)
        rows += [s for s in range(NB) if s not in rows]
        if n + 1 == len(COLUMNS):
            multiply(rows, cols)
        else:
            at = min(fresh, NB - LEAD)
            multiply(rows[:at], cols)
            held_back = len(pe_steps)
            multiply(rows[at:fresh], cols)
            read_rows(COLUMNS[n + 1])
            degrees = [step for step in pe_steps if step[0] == "degree" and step[1] in COLUMNS[n + 1]]
            pe_steps[:] = [step for step in pe_steps if step not in degrees]
            pe_steps[held_back:held_back] = degrees
            multiply(rows[fresh:], cols)
        kept -= {(s, t) for s, t in kept if t <= cols[-1]}
    assert len(read) == NB * NB

    loads = []
    free = [(0.0, n) for n in range(SLOTS)]
    now, pe, last_first = 0.0, 0.0, {}
    ready, slot_of, load_at = {}, {}, {}
    todo = list(pe_steps)
    vector, pool, products, done_at = [], [], [], {}

    def run_pe():
        nonlocal pe
        while todo:
            step = todo[0]
            if step[0] == "degree":
                if step[1] not in last_first:
                    return
                t0 = last_first[step[1]] + SUMS
                for t in sorted(t for t in col_read if t < first_col[step[1]]):
                    vector.append((max(col_read.pop(t) + SUMS, t0 - 1.5), "column_sum", t))
                vector.append((t0 - 1.0, "row_base", step[1]))
                vector.append((t0, "row_sum", step[1]))
                pe = max(pe, t0 + 0.5) + 0.3
                vector.append((pe + 0.1, "degree", step[1]))
                pool.append((pe + 0.5, "power", step[1]))
                vector.append((pe + 1.0, "scale", step[1]))
                done_at[step[1]] = pe + 2.5
            else:
                _, s, cols = step
                if any((s, t) not in ready for t in cols) or any(t not in done_at for t in cols):
                    return
                for t in cols:
                    pe = max(pe, ready[s, t], done_at[t])
                    vector.append((max(ready[s, t], pe - AHEAD) - TURN, "turn", load_at[s, t]))
                    pe += PRODUCT
                    free.append((pe, slot_of[s, t]))
                vector.append((pe + 0.1, "add", len(products)))
                products.append((s, cols))
                if cols[-1] == NB - 1:
                    vector.append((pe + FINISH, "finish", s))
            todo.pop(0)

    read_of, act, col_read = [0] * NB, [], {}
    last_cols = COLUMNS[-1]
    end_from = order.index(next(o for o in order if o[1] == last_cols[0] and o[2] > COLUMNS[-2][-1]))
    for at, (kind, s, t) in enumerate(order):
        usable = SLOTS - LATE if at >= end_from or (kind != "sum_only" and t in last_cols) else SLOTS
        assert any(slot < usable for _, slot in free), "more tiles are kept than fit"
        freed, slot = min(f for f in free if f[1] < usable)
        free.remove((freed, slot))
        now = max(now, freed) + LOAD
        k = len(loads)
        loads.append((kind, s, t, slot))
        if kind == "stream":
            col_read[t] = now
        if kind != "again":
            read_of[s] += 1
            if read_of[s] == NB:
                last_first[s] = now
        if kind != "again":
            n = sum(how != "again" for how, *_ in loads)
            if n % POOL_OF[1] < POOL_OF[0] or s == t:
                pool.append((now, "sum", k))
                vector.append((now + 3.9, "quarters", k))
            else:
                act.append(k)
        if kind == "sum_only":
            free.append((now + SUMS, slot))
        else:
            wait = now + (0.2 if kind == "again" else SUMS)
            ready[s, t], slot_of[s, t], load_at[s, t] = wait + TURN, slot, k
        run_pe()
    assert not todo
    return loads, pe_steps, products, act, *([v[1:] for v in sorted(e, key=lambda v: v[0])] for e in (vector, pool))


def gcn_resnorm(nc: bass.Bass, x: bass.AP, adj: bass.AP, w: bass.AP, out: bass.AP):
    fp32 = mybir.dt.float32
    ALU = mybir.AluOpType
    ACT = mybir.ActivationFunctionType
    AX = mybir.AxisListType

    loads, pe_steps, products, on_act, vector_steps, pool_steps = plan()
    column_end = {t: n + 1 for n, (s, cols) in enumerate(products) for t in cols}
    first_reads = [k for k, (kind, *_) in enumerate(loads) if kind != "again"]
    first_col = {t: cols[0] for cols in COLUMNS for t in cols}
    with_row = {k for k in first_reads if loads[k][2] >= first_col[loads[k][1]]}
    far_from = {r: min([loads[k][2] for k in with_row if loads[k][:2] == ("sum_only", r)], default=NB) for r in range(NB)}
    last_read = {s: k for k, (kind, s, *_) in enumerate(loads) if kind != "again"}
    x_after = {k - 3: s for s, k in last_read.items()}
    pool_nth = {k: n + 1 for n, k in enumerate(k for kind, k in pool_steps if kind == "sum")}
    act_nth = {k: n + 1 for n, k in enumerate(on_act)}
    turned = [k for kind, k in vector_steps if kind == "turn"]
    turn_nth = {k: n + 1 for n, k in enumerate(turned)}
    load_of = {(s, t): k for k, (kind, s, t, _) in enumerate(loads) if kind != "sum_only"}
    product_of = {(s, t): n for n, (s, cols) in enumerate(products) for t in cols}
    degree_nth = {r: n + 1 for n, r in enumerate(r for kind, r, *_ in pe_steps if kind == "degree")}
    finished = [s for s, cols in products if cols[-1] == NB - 1]
    final_of = {s: n for n, (s, cols) in enumerate(products) if cols[-1] == NB - 1}
    arrived, counts = [], [0] * SLOTS
    before = []
    last_in = {}
    for k, (kind, _, _, slot) in enumerate(loads):
        counts[slot] += 16 if kind == "sum_only" else 16 * Q
        arrived.append(counts[slot])
        before.append(last_in.get(slot))
        last_in[slot] = k

    RING = G // CH
    BANKS = 5

    with ExitStack() as ctx:
        def sb(name, shape):
            return ctx.enter_context(nc.sbuf_tensor(name, shape, fp32))

        def pb(name, shape):
            return ctx.enter_context(nc.psum_tensor(name, shape, fp32))

        def sem(name):
            return ctx.enter_context(nc.semaphore(name))

        tiles = [sb(f"tile{n}", [128, G, 128]) for n in range(SLOTS)]
        xs = sb("xs", [128, XRING, CH, F])
        hT = sb("hT", [128, NB, CH, Q, 32])
        row_part = sb("row_part", [128, 2, NB, G])
        far_part = sb("far_part", [128, 2, NB, Q])
        far = sb("far", [128, Q])
        base = sb("base", [128, Q, CH])
        in_quadrant = sb("in_quadrant", [128, CH])
        col_part = sb("col_part", [128, 2, NB, G])
        sums = sb("sums", [128, NB, G])
        halves = sb("halves", [128, G, 64])
        quarters = sb("quarters", [128, 2, G, 32])
        rsum = sb("rsum", [128, 2, G])
        deg = sb("deg", [128, CH])
        power = sb("power", [128, CH])
        d = sb("d", [128, NB, CH])
        same = sb("same", [128, Q, 32])
        ident = sb("ident", [128, Q, 32])
        w_sb = sb("w_sb", [F, F])
        res, pos, neg = (tiles[SLOTS - LATE + n][:, :, :].rearrange("p (n b) f -> p n b f", n=RING) for n in range(LATE))
        stats = sb("stats", [128, CH, 6])
        mv = sb("mv", [128, RING, CH, 2])
        var_eps = sb("var_eps", [128, CH])
        rstd = sb("rstd", [128, RING, CH])

        p_prod = [pb(f"p_prod{n}", [128, B]) for n in range(BANKS)]
        p_deg = pb("p_deg", [128, B])
        p_out = [pb(f"p_out{n}", [128, CH, F]) for n in range(2)]

        x_loaded = [sem(f"x_loaded{n}") for n in range(2)]
        w_loaded = sem("w_loaded")
        loaded = [sem(f"loaded{n}") for n in range(SLOTS)]
        res_loaded = [sem(f"res_loaded{n}") for n in range(RING)]
        cleared = sem("cleared")
        consts = sem("consts")
        act_summed = sem("act_summed")
        pool_summed = sem("pool_summed")
        pool_step = sem("pool_step")
        pool_halved = sem("pool_halved")
        quarters_summed = sem("quarters_summed")
        tile_turned = sem("tile_turned")
        base_step = sem("base_step")
        base_ready = sem("base_ready")
        row_read = sem("row_read")
        row_summed = sem("row_summed")
        col_summed = sem("col_summed")
        degree_out = sem("degree_out")
        deg_ready = sem("deg_ready")
        d_ready = sem("d_ready")
        var_ready = sem("var_ready")
        xs_ready = sem("xs_ready")
        product_out = sem("product_out")
        product_added = sem("product_added")
        hw_out = sem("hw_out")
        relu_neg = sem("relu_neg")
        exp_ready = sem("exp_ready")
        relu_pos = sem("relu_pos")
        z_ready = sem("z_ready")
        elu_ready = sem("elu_ready")
        y_ready = sem("y_ready")
        stats_ready = sem("stats_ready")
        mv_ready = sem("mv_ready")
        rstd_ready = sem("rstd_ready")
        normed = sem("normed")
        stored = [sem(f"stored{n}") for n in range(RING)]

        block = ctx.enter_context(nc.Block())

        adj_v = adj.rearrange("(s g i) (t q c) -> s t q i g c", g=G, i=32, q=Q, c=128)
        adj_rows = adj.rearrange("(s k p) (t c) -> s t p k c", k=Q, p=128, c=B)
        x_v = x.rearrange("(t q b j) f -> t q j b f", q=Q, b=CH, j=32)
        out_v = out.rearrange("(t q b j) f -> t q j b f", q=Q, b=CH, j=32)

        def quadrant(q):
            return slice(32 * q, 32 * q + 32)

        def as_rows(buffer):
            return buffer[:, :, :].rearrange("p (k g) c -> p k (g c)", k=Q)

        def sum_at(k):
            kind, s, t, _ = loads[k]
            if kind == "sum_only":
                return far_part[:, s % 2, t]
            return row_part[:, s % 2, t] if k in with_row else col_part[:, t % 2, s]

        def of_rows(kind, buffer):
            return buffer.rearrange("p (k g) c -> p k (g c)", k=Q) if kind == "sum_only" else buffer

        def wait_sum_free(engine, k):
            _, s, t, _ = loads[k]
            if k in with_row and s >= 2:
                engine.wait_ge(row_summed, s - 1)
            if k not in with_row and t >= 2:
                engine.wait_ge(col_summed, t - 1)

        @block.sync
        def _(sp):
            sp.dma_start(w_sb[:, :], w).then_inc(w_loaded, 16)
            for k, (kind, s, t, slot) in enumerate(loads):
                if before[k] is not None:
                    was, s0, t0, _ = loads[before[k]]
                    if was == "sum_only":
                        if before[k] in act_nth:
                            sp.wait_ge(act_summed, act_nth[before[k]])
                        else:
                            sp.wait_ge(pool_summed, pool_nth[before[k]])
                    else:
                        sp.wait_ge(product_out, product_of[s0, t0] + 1)
                if kind == "sum_only":
                    sp.dma_start(as_rows(tiles[slot]), adj_rows[s, t]).then_inc(loaded[slot], 16)
                else:
                    for q in range(Q):
                        sp.dma_start(tiles[slot][quadrant(q)], adj_v[s, t, q]).then_inc(loaded[slot], 16)
                if k in x_after:
                    r = x_after[k]
                    if r >= 2:
                        sp.wait_ge(xs_ready, r - 1)
                    if r >= XRING:
                        sp.wait_ge(product_out, column_end[r - XRING])
                    for q in range(Q):
                        sp.dma_start(xs[quadrant(q), r % XRING], x_v[r, q]).then_inc(x_loaded[r % 2], 16)

        @block.gpsimd
        def _(pool):
            nc.gpsimd.memset(same[:, :, :], 0.0).then_inc(cleared, 1)
            nc.gpsimd.memset(ident[:, :, :], 0.0).then_inc(cleared, 1)
            pool.wait_ge(cleared, 2)
            nc.gpsimd.affine_select(out=ident[:, :, :], in_=ident[:, :, :], compare_op=ALU.not_equal, fill=1.0,
                                    base=0, pattern=[[-32, Q], [-1, 32]], channel_multiplier=1).then_inc(consts, 1)
            for q in range(Q):
                if q:
                    pool.wait_ge(consts, q + 1)
                nc.gpsimd.affine_select(out=same[:, :, :], in_=same[:, :, :], compare_op=ALU.not_equal, fill=1.0,
                                        base=-32 * q, pattern=[[0, Q], [-1, 32]],
                                        channel_multiplier=1).then_inc(consts, 1)
            pool.wait_ge(consts, 1 + Q)
            nc.gpsimd.memset(power[:, :], -0.5).then_inc(consts, 1)
            pool.wait_ge(consts, 2 + Q)
            steps = 0
            for kind, k in pool_steps:
                if kind == "power":
                    r = k
                    pool.wait_ge(deg_ready, degree_nth[r])
                    nc.gpsimd.tensor_tensor(d[:, r], deg[:, :], power[:, :], ALU.pow).then_inc(d_ready, 1)
                    continue
                how, s, t, slot = loads[k]
                tile = tiles[slot]
                pool.wait_ge(loaded[slot], arrived[k])
                if s == t:
                    diag = tile[:, :, :].rearrange("p (q b) c -> p b q c", q=Q)
                    for b in range(CH):
                        nc.gpsimd.tensor_tensor(diag[:, b, :, 32 * b:32 * b + 32], diag[:, b, :, 32 * b:32 * b + 32],
                                                ident[:, :, :], ALU.add).then_inc(pool_step, 1)
                    steps += CH
                    pool.wait_ge(pool_step, steps)
                if pool_nth[k] > 1:
                    pool.wait_ge(pool_summed, pool_nth[k] - 1)
                nth = pool_nth[k]
                view = as_rows(tile) if how == "sum_only" else tile[:, :, :]
                half, quarter = of_rows(how, halves[:, :, :]), of_rows(how, quarters[:, nth % 2])
                c = view.shape[-1] // 2
                nc.gpsimd.tensor_tensor(half, view[:, :, 0:c], view[:, :, c:2 * c], ALU.add).then_inc(pool_halved, 1)
                pool.wait_ge(pool_halved, nth)
                if nth > 2:
                    pool.wait_ge(quarters_summed, nth - 2)
                nc.gpsimd.tensor_tensor(quarter, half[:, :, 0:c // 2], half[:, :, c // 2:c], ALU.add)\
                  .then_inc(pool_summed, 1)

            def inverse_deviation(n):
                pool.wait_ge(mv_ready, n + 1)
                nc.gpsimd.tensor_scalar(var_eps[:, :], mv[:, n % RING, :, 1], EPS, None, ALU.add).then_inc(var_ready, 1)
                pool.wait_ge(var_ready, n + 1)
                if n >= 3:
                    pool.wait_ge(normed, n - 2)
                nc.gpsimd.tensor_tensor(rstd[:, n % RING], var_eps[:, :], power[:, :], ALU.pow).then_inc(rstd_ready, 1)
                pool.wait_ge(rstd_ready, n + 1)

            def add_residual(n):
                pool.wait_ge(elu_ready, n + 1)
                pool.wait_ge(res_loaded[n % RING], 64 * (n // RING + 1))
                nc.gpsimd.tensor_tensor(pos[:, n % RING], pos[:, n % RING], res[:, n % RING], ALU.add).then_inc(y_ready, 1)

            for n in range(NB):
                if n >= 1:
                    inverse_deviation(n - 1)
                add_residual(n)
            inverse_deviation(NB - 1)

        @block.scalar
        def _(act):
            for k in on_act:
                kind, s, t, slot = loads[k]
                act.wait_ge(loaded[slot], arrived[k])
                wait_sum_free(act, k)
                view = as_rows(tiles[slot]) if kind == "sum_only" else tiles[slot]
                for g in range(view.shape[1]):
                    ins = nc.scalar.activation(view[:, g], view[:, g], ACT.Copy, accum_out=sum_at(k)[:, g:g + 1])
                ins.then_inc(act_summed, 1)

            def load_residual(n):
                for q in range(Q):
                    act.dma_start(res[quadrant(q), n % RING], x_v[finished[n], q]).then_inc(res_loaded[n % RING], 16)

            def store(n):
                s = finished[n]
                act.wait_ge(normed, n + 1)
                if n + RING < NB:
                    load_residual(n + RING)
                for q in range(Q):
                    act.dma_start(out_v[s, q], pos[quadrant(q), n % RING]).then_inc(stored[n % RING], 16)

            act.wait_ge(product_out, final_of[finished[0]])
            for n in range(RING):
                load_residual(n)
            for n in range(NB):
                act.wait_ge(hw_out, n + 1)
                if n >= RING:
                    act.wait_ge(stored[n % RING], 64 * (n // RING))
                for b in range(CH):
                    ins = nc.scalar.activation(pos[:, n % RING, b], p_out[n % 2][:, b], ACT.Copy,
                                               scale=d[:, finished[n], b:b + 1])
                ins.then_inc(z_ready, 1)
                act.wait_ge(z_ready, n + 1)
                nc.scalar.activation(neg[:, n % RING], pos[:, n % RING], ACT.Relu, scale=-1.0).then_inc(relu_neg, 1)
                act.wait_ge(relu_neg, n + 1)
                nc.scalar.activation(pos[:, n % RING], pos[:, n % RING], ACT.Relu).then_inc(relu_pos, 1)
                nc.scalar.activation(neg[:, n % RING], neg[:, n % RING], ACT.Exp, scale=-1.0).then_inc(exp_ready, 1)
                if n >= 2:
                    store(n - 2)
            store(NB - 2)
            store(NB - 1)
            for n in range(RING):
                act.wait_ge(stored[n], 64 * len(range(n, NB, RING)))

        @block.tensor
        def _(pe):
            def out_rows(n):
                s = finished[n]
                if n >= 2:
                    pe.wait_ge(z_ready, n - 1)
                for b in range(CH):
                    ins = nc.tensor.matmul(p_out[n % 2][:, b], hT[:, s, b], w_sb[:, :], start=True, stop=True)
                ins.then_inc(hw_out, 1)

            pe.wait_ge(consts, 2 + Q)
            pe.wait_ge(w_loaded, 16)
            nth = 0
            finals = 0
            for kind, s, *rest in pe_steps:
                if kind == "degree":
                    pe.wait_ge(row_summed, degree_nth[s])
                    if degree_nth[s] > 1:
                        pe.wait_ge(deg_ready, degree_nth[s] - 1)
                    for q in range(Q):
                        ins = nc.tensor.matmul(p_deg[quadrant(q), 0:CH], same[:, q], rsum[:, degree_nth[s] % 2, CH * q:CH * q + CH],
                                               start=True, stop=True)
                    ins.then_inc(degree_out, 1)
                    continue
                cols = rest[0]
                if nth >= BANKS:
                    pe.wait_ge(product_added, nth - BANKS + 1)
                for t in cols:
                    pe.wait_ge(xs_ready, degree_nth[t])
                    pe.wait_ge(tile_turned, turn_nth[load_of[s, t]])
                    tile = tiles[loads[load_of[s, t]][3]]
                    chunks = tile[:, :, :].rearrange("p g (b i) -> p b g i", b=CH)
                    for b in range(CH):
                        ins = nc.tensor.matmul(p_prod[nth % BANKS][:, :].rearrange("f (g i) -> f g i", g=G),
                                               xs[:, t % XRING, b], chunks[:, b],
                                               start=(t == cols[0] and b == 0), stop=(t == cols[-1] and b == CH - 1))
                ins.then_inc(product_out, 1)
                nth += 1
                if cols[-1] == NB - 1:
                    finals += 1
                    if finals > LAG:
                        pe.wait_ge(product_added, final_of[finished[finals - 1 - LAG]] + 1)
                        out_rows(finals - 1 - LAG)
            for n in range(NB - LAG, NB):
                pe.wait_ge(product_added, final_of[finished[n]] + 1)
                out_rows(n)

        @block.vector
        def _(dve):
            def elu(n):
                dve.wait_ge(relu_pos, n + 1)
                dve.wait_ge(exp_ready, n + 1)
                nc.vector.scalar_tensor_tensor(out=pos[:, n % RING], in0=neg[:, n % RING], scalar=-1.0, in1=pos[:, n % RING],
                                               op0=ALU.add, op1=ALU.add).then_inc(elu_ready, 1)

            def statistics(n):
                dve.wait_ge(y_ready, n + 1)
                if n >= 3:
                    dve.wait_ge(var_ready, n - 2)
                for b in range(CH):
                    ins = nc.vector.bn_stats(stats[:, b], pos[:, n % RING, b])
                ins.then_inc(stats_ready, 1)
                dve.wait_ge(stats_ready, n + 1)
                for b in range(CH):
                    ins = nc.vector.bn_aggr(mv[:, n % RING, b], stats[:, b])
                ins.then_inc(mv_ready, 1)

            def normalise(n):
                dve.wait_ge(rstd_ready, n + 1)
                for b in range(CH):
                    ins = nc.vector.tensor_scalar(pos[:, n % RING, b], pos[:, n % RING, b], mv[:, n % RING, b, 0:1],
                                                  rstd[:, n % RING, b:b + 1], ALU.subtract, ALU.mult)
                ins.then_inc(normed, 1)

            def wait_sums(dve, ks):
                if any(k in act_nth for k in ks):
                    dve.wait_ge(act_summed, max(act_nth[k] for k in ks if k in act_nth))
                if any(k in pool_nth for k in ks):
                    dve.wait_ge(quarters_summed, max(pool_nth[k] for k in ks if k in pool_nth))

            dve.wait_ge(consts, 2 + Q)
            nc.vector.tensor_reduce(in_quadrant[:, :], ident[:, :, :], AX.X, ALU.add).then_inc(base_step, 1)
            dve.wait_ge(base_step, 1)
            base_steps = 1
            finish_nth = 0
            for kind, arg in vector_steps:
                if kind == "turn":
                    k = arg
                    how, s, t, slot = loads[k]
                    if how == "again":
                        dve.wait_ge(loaded[slot], arrived[k])
                    elif k in act_nth:
                        dve.wait_ge(act_summed, act_nth[k])
                    else:
                        dve.wait_ge(pool_summed, pool_nth[k])
                    nc.vector.transpose(tiles[slot][:, :, :], tiles[slot][:, :, :]).then_inc(tile_turned, 1)
                elif kind == "quarters":
                    how, s, t, _ = loads[arg]
                    dve.wait_ge(pool_summed, pool_nth[arg])
                    wait_sum_free(dve, arg)
                    nc.vector.tensor_reduce(sum_at(arg), of_rows(how, quarters[:, pool_nth[arg] % 2]), AX.X, ALU.add)\
                      .then_inc(quarters_summed, 1)
                elif kind == "row_base":
                    r = arg
                    nth = degree_nth[r]
                    if nth > 1:
                        dve.wait_ge(row_summed, nth - 1)
                    only = [k for k in with_row if loads[k][1] == r and loads[k][0] == "sum_only"]
                    wait_sums(dve, only)
                    if r > 0:
                        dve.wait_ge(col_summed, first_col[r])
                    if only:
                        nc.vector.tensor_reduce(far[:, :], far_part[:, r % 2, far_from[r]:].rearrange("p t k -> p k t"),
                                                AX.X, ALU.add).then_inc(base_step, 1)
                        base_steps += 1
                        dve.wait_ge(base_step, base_steps)
                        ins = nc.vector.tensor_tensor(base[:, :, :], far[:, :].unsqueeze(2).to_broadcast([128, Q, CH]),
                                                      in_quadrant[:, :].unsqueeze(1).to_broadcast([128, Q, CH]), ALU.mult)
                        if r > 0:
                            ins.then_inc(base_step, 1)
                            base_steps += 1
                            dve.wait_ge(base_step, base_steps)
                            ins = nc.vector.tensor_tensor(base[:, :, :], base[:, :, :],
                                                          sums[:, r].rearrange("p (q b) -> p q b", q=Q), ALU.add)
                    else:
                        ins = nc.vector.tensor_copy(base[:, :, :], sums[:, r].rearrange("p (q b) -> p q b", q=Q))
                    ins.then_inc(base_ready, 1)
                elif kind == "row_sum":
                    r = arg
                    nth = degree_nth[r]
                    wait_sums(dve, [k for k in with_row if loads[k][1] == r])
                    if nth > 2:
                        dve.wait_ge(degree_out, nth - 2)
                    own = row_part[:, r % 2, first_col[r]:far_from[r]].rearrange("p t g -> p g t")
                    nc.vector.tensor_reduce(rsum[:, nth % 2], own, AX.X, ALU.add).then_inc(row_read, 1)
                    dve.wait_ge(row_read, nth)
                    dve.wait_ge(base_ready, nth)
                    nc.vector.tensor_tensor(rsum[:, nth % 2], rsum[:, nth % 2],
                                            base[:, :, :].rearrange("p q b -> p (q b)"), ALU.add).then_inc(row_summed, 1)
                elif kind == "column_sum":
                    t = arg
                    wait_sums(dve, [k for k in first_reads if k not in with_row and loads[k][2] == t])
                    if t == 0:
                        nc.vector.tensor_copy(sums[:, 1:], col_part[:, 0, 1:]).then_inc(col_summed, 1)
                    else:
                        dve.wait_ge(col_summed, t)
                        nc.vector.tensor_tensor(sums[:, t + 1:], sums[:, t + 1:], col_part[:, t % 2, t + 1:], ALU.add)\
                          .then_inc(col_summed, 1)
                elif kind == "degree":
                    r = arg
                    nth = degree_nth[r]
                    dve.wait_ge(degree_out, nth)
                    if nth > 1:
                        dve.wait_ge(d_ready, nth - 1)
                    nc.vector.tensor_copy(deg[:, :], p_deg[:, 0:CH]).then_inc(deg_ready, 1)
                elif kind == "scale":
                    r = arg
                    nth = degree_nth[r]
                    dve.wait_ge(d_ready, nth)
                    dve.wait_ge(x_loaded[r % 2], 16 * Q * (r // 2 + 1))
                    for b in range(CH):
                        ins = nc.vector.tensor_scalar(xs[:, r % XRING, b], xs[:, r % XRING, b], d[:, r, b:b + 1], None, ALU.mult)
                    ins.then_inc(xs_ready, 1)
                elif kind == "add":
                    n = arg
                    s, cols = products[n]
                    dve.wait_ge(product_out, n + 1)
                    rows = hT[:, s].rearrange("f b q i -> f q b i")
                    product = p_prod[n % BANKS][:, :].rearrange("f (q b i) -> f q b i", q=Q, b=CH)
                    if cols[0] == 0:
                        nc.vector.tensor_copy(rows, product).then_inc(product_added, 1)
                    else:
                        nc.vector.tensor_tensor(rows, product, rows, ALU.add).then_inc(product_added, 1)
                else:
                    if finish_nth >= 2:
                        normalise(finish_nth - 2)
                    if finish_nth >= 1:
                        statistics(finish_nth - 1)
                    elu(finish_nth)
                    finish_nth += 1
            normalise(NB - 2)
            statistics(NB - 1)
            normalise(NB - 1)


def kernel(x, adj, L0_gnn_w):
    import numpy as _np
    import concourse.bacc as _bacc
    from concourse import mybir as _mybir
    from concourse.bass_utils import run_bass_kernel_spmd as _run

    nc = _bacc.Bacc("TRN2", target_bir_lowering=False, num_devices=1, dynamic_dma_scratch_size=256)
    arrays, args = {}, []
    for name, a in (("x", x), ("adj", adj), ("w", L0_gnn_w)):
        a = _np.ascontiguousarray(a)
        arrays[f"in_{name}"] = a
        args.append(nc.dram_tensor(f"in_{name}", a.shape, _mybir.dt.from_np(a.dtype), kind="ExternalInput").ap())
    args.append(nc.dram_tensor("out_rows", (N, F), _mybir.dt.float32, kind="ExternalOutput").ap())
    gcn_resnorm(nc, *args)
    return _run(nc, [arrays], core_ids=[0]).results[0]["out_rows"]
```
